# Optimizing a Trainium2 kernel written in Bass

```python
import numpy as np
import jax
import jax.numpy as jnp

def _softmax(x, axis=-1):
    return jax.nn.softmax(x, axis=axis)

def _gelu(x):
    return jax.nn.gelu(x, approximate=True)

def _silu(x):
    return jax.nn.silu(x)

def _sigmoid(x):
    return jax.nn.sigmoid(x)

def _layernorm(x, axis=-1, eps=1e-05):
    m = jnp.mean(x, axis=axis, keepdims=True)
    v = jnp.var(x, axis=axis, keepdims=True)
    return (x - m) / jnp.sqrt(v + eps)

def _scatter_add(tgt, idx, src, axis=0):
    return tgt.at[idx].add(src)

def _segment_sum(src, seg, n):
    return jax.ops.segment_sum(src, seg, n)
kernel_name = 'mk_gnn_preln_d2_gnn_r8_128614'

def setup_inputs(seed: int=0):
    np.random.seed(seed)
    _w = jnp.asarray

    def _rec_inputs():
        import jax
        import jax.numpy as jnp
        _gk = jax.random.key(seed)
        x = -0.0005121 + 1.001 * jax.random.normal(jax.random.fold_in(_gk, 1), (12500, 64), jnp.float32)
        src = jax.random.randint(jax.random.fold_in(_gk, 2), (400000,), 0, 12500, jnp.int32)
        dst = jax.random.randint(jax.random.fold_in(_gk, 3), (400000,), 0, 12500, jnp.int32)
        _o = jnp.argsort(dst, stable=True)
        src = src[_o]
        dst = dst[_o]
        edge_attr_16 = 0.000196303 + 1.00016 * jax.random.normal(jax.random.fold_in(_gk, 12), (400000, 16), jnp.float32)
        edge_type_16 = jax.random.randint(jax.random.fold_in(_gk, 14), (400000,), 0, 16, jnp.int32)
        return (x, src, dst, edge_attr_16, edge_type_16)
    x, src, dst, edge_attr_16, edge_type_16 = _rec_inputs()

    def _L0_gnn_setup():
        import jax, jax.numpy as jnp
        import numpy as np
        N_NODES = 6250
        N_EDGES = 100000
        D_IN = 64
        D_OUT = 64
        NUM_RELS = 16
        key = jax.random.key(seed)
        k1, k2, k3, k4, k5 = jax.random.split(key, 5)
        feat = jax.random.normal(k1, (N_NODES, D_IN), dtype=jnp.float32)
        weight = jax.random.normal(k2, (NUM_RELS, D_IN, D_OUT), dtype=jnp.float32) * 0.05
        src = jax.random.randint(k3, (N_EDGES,), 0, N_NODES, dtype=jnp.int32)
        dst = jax.random.randint(k4, (N_EDGES,), 0, N_NODES, dtype=jnp.int32)
        etypes = jax.random.randint(k5, (N_EDGES,), 0, NUM_RELS, dtype=jnp.int32)
        return {'feat': feat, 'weight': weight, 'src': src, 'dst': dst, 'etypes': etypes}
    _L0_gnn_all = _L0_gnn_setup()
    _L0_gnn_in = {k: v for k, v in _L0_gnn_all.items() if k in ('weight',)}
    del _L0_gnn_all

    def _L1_gnn_setup():
        import jax, jax.numpy as jnp
        import numpy as np
        N_NODES = 12500
        N_EDGES = 200000
        IN_CH = 64
        OUT_CH = 64
        EDGE_DIM = 16
        key = jax.random.key(seed)
        ks = jax.random.split(key, 8)
        x = jax.random.normal(ks[0], (N_NODES, IN_CH), dtype=jnp.float32)
        edge_index = jax.random.randint(ks[1], (2, N_EDGES), 0, N_NODES, dtype=jnp.int64)
        edge_attr = jax.random.normal(ks[2], (N_EDGES, EDGE_DIM), dtype=jnp.float32)
        W_l = jax.random.normal(ks[3], (IN_CH, OUT_CH), dtype=jnp.float32) / np.sqrt(IN_CH)
        b_l = jnp.zeros((OUT_CH,), dtype=jnp.float32)
        W_r = jax.random.normal(ks[4], (IN_CH, OUT_CH), dtype=jnp.float32) / np.sqrt(IN_CH)
        W_e = jax.random.normal(ks[5], (EDGE_DIM, OUT_CH), dtype=jnp.float32) / np.sqrt(EDGE_DIM)
        b_e = jax.random.normal(ks[6], (OUT_CH,), dtype=jnp.float32) * 0.01
        return {'x': x, 'edge_index': edge_index, 'edge_attr': edge_attr, 'W_l': W_l, 'b_l': b_l, 'W_r': W_r, 'W_e': W_e, 'b_e': b_e}
    _L1_gnn_all = _L1_gnn_setup()
    _L1_gnn_in = {k: v for k, v in _L1_gnn_all.items() if k in ('W_l', 'b_l', 'W_r', 'W_e', 'b_e')}
    del _L1_gnn_all
    return {'x': x, 'src': src, 'dst': dst, 'edge_attr_16': edge_attr_16, 'edge_type_16': edge_type_16, 'L0_gnn_weight': _L0_gnn_in['weight'], 'L1_gnn_W_l': _L1_gnn_in['W_l'], 'L1_gnn_b_l': _L1_gnn_in['b_l'], 'L1_gnn_W_r': _L1_gnn_in['W_r'], 'L1_gnn_W_e': _L1_gnn_in['W_e'], 'L1_gnn_b_e': _L1_gnn_in['b_e']}

def reference(x, src, dst, edge_attr_16, edge_type_16, L0_gnn_weight, L1_gnn_W_l, L1_gnn_b_l, L1_gnn_W_r, L1_gnn_W_e, L1_gnn_b_e):
    import jax
    import jax.numpy as jnp

    def _L0_gnn_ref(feat, weight, src, dst, etypes):
        import jax, jax.numpy as jnp
        import numpy as np
        N_NODES = 6250
        N_EDGES = 100000
        D_IN = 64
        D_OUT = 64
        NUM_RELS = 16
        num_rels = weight.shape[0]
        h_src = feat[src]
        msg = jnp.zeros((h_src.shape[0], weight.shape[2]), dtype=feat.dtype)
        for r in range(num_rels):
            mask = etypes == r
            msg = msg + h_src * mask[:, None].astype(feat.dtype) @ weight[r]
        out = jax.ops.segment_sum(msg, dst, num_segments=feat.shape[0])
        return out

    def _L1_gnn_ref(x, edge_index, edge_attr, W_l, b_l, W_r, W_e, b_e):
        import jax, jax.numpy as jnp
        import numpy as np
        N_NODES = 12500
        N_EDGES = 200000
        IN_CH = 64
        OUT_CH = 64
        EDGE_DIM = 16
        N = x.shape[0]
        row, col = (edge_index[0], edge_index[1])
        x_j = x[row]
        agg = jax.ops.segment_sum(x_j, col, num_segments=N)
        cnt = jax.ops.segment_sum(jnp.ones((row.shape[0],), x.dtype), col, num_segments=N)
        mean = agg / jnp.maximum(cnt, 1.0)[:, None]
        out = mean @ W_l + b_l + x @ W_r
        e = edge_attr @ W_e + b_e
        out = out + jnp.zeros_like(out).at[col].set(e)
        return out
    edge_index = jnp.stack([src, dst])
    h = jnp.maximum(_layernorm(x, axis=-1), 0.0)
    x = x + _L0_gnn_ref(h, L0_gnn_weight, src, dst, edge_type_16)
    h = jnp.maximum(_layernorm(x, axis=-1), 0.0)
    x = x + _L1_gnn_ref(h, edge_index, edge_attr_16, L1_gnn_W_l, L1_gnn_b_l, L1_gnn_W_r, L1_gnn_W_e, L1_gnn_b_e)
    return x

_drawn_inputs = setup_inputs


def setup_inputs(seed=0):
    import zlib

    import numpy as np

    out = dict(_drawn_inputs(seed))
    spreads = {'L1_gnn_b_l': (0.0, 0.1)}
    factors = {'L1_gnn_b_e': 8.0}
    for name, (base, spread) in spreads.items():
        noise = np.random.default_rng([zlib.crc32(name.encode()), seed]).standard_normal(out[name].shape)
        drawn = base * np.exp(spread * noise) if base else spread * noise
        out[name] = jnp.asarray(drawn.astype(out[name].dtype))
    for name, factor in factors.items():
        out[name] = (out[name] * factor).astype(out[name].dtype)
    return out
```

```python
from contextlib import ExitStack

import concourse.bass as bass
from concourse import mybir

ALU = mybir.AluOpType
ACT = mybir.ActivationFunctionType
AX = mybir.AxisListType.X
F32 = mybir.dt.float32
I32 = mybir.dt.int32
U32 = mybir.dt.uint32

P = 128
G = 5
NG = 5
K = G * NG
WIN = 128
TB = 7
EPS = 1e-5


def gnn_two_layers(nc, x, src, dst, edge_attr, edge_type, w_rel, w_l, b_l, w_r, w_e, b_e, out):
    N, D = x.shape
    E = src.shape[0]
    R = w_rel.shape[0]
    A = edge_attr.shape[1]
    S = E // (P * K)
    NT = -(-N // P)
    NN = NT * P
    FULL = N // NT
    PART = N - FULL * NT
    SPRAY = FULL // 16 * 16
    NB = NT // TB
    CNT = D
    M0 = D + 1 + A
    HALF = R * D // 2
    assert S * P * K == E and NB * TB == NT and NB % 2 == 0 and HALF == 512
    assert FULL == P - 1 and S <= P and WIN == P

    table0 = nc.dram_tensor("rel_table", (NN * R, D), F32, kind="Internal").ap()
    table1 = nc.dram_tensor("h_table", (NN, D), F32, kind="Internal").ap()

    with ExitStack() as ctx:
        def sb(name, shape, dt=F32):
            return ctx.enter_context(nc.sbuf_tensor(name, shape, dt))

        def sem(name):
            return ctx.enter_context(nc.semaphore(name))

        sum0 = sb("sum0", [P, NN + WIN])
        sum1 = sb("sum1", [P, NN + WIN])
        x_sb = sb("x_sb", [P, NT, D])
        idx = sb("idx", [P, S, K], I32)
        rel = sb("rel", [P, S, K])
        last = sb("last", [P, S, K])
        msg = sb("msg", [P, K, M0])
        onehot = sb("onehot", [P, K, WIN])
        attr = sb("attr", [P, K, A])
        istage = sb("istage", [P, K], I32)
        iota_i = sb("iota_i", [P, WIN], I32)
        iota_c = sb("iota_c", [P, 1], I32)
        iota = sb("iota", [P, WIN])
        iota_w = sb("iota_w", [P, WIN])
        icol = sb("icol", [P, 1])
        ident = sb("ident", [P, P])
        upper = sb("upper", [P, P])
        nxt = sb("nxt", [P, S], I32)
        mnp = sb("mnp", [P, S])
        mxp = sb("mxp", [P, S])
        col = sb("col", [P, 8])
        coli = sb("coli", [P, 4], I32)
        steps = sb("steps", [1, S, 4], I32)
        wrel = sb("wrel", [P, R, D])
        wl = sb("wl", [P, D])
        wcomb = sb("wcomb", [P, D])
        bl = sb("bl", [P, D])
        eps = sb("eps", [P, 1])
        ones = sb("ones", [P, P])
        bc = sb("bc", [P, 2, P])
        stat = sb("stat", [P, 2, 3, TB])
        cen = sb("cen", [P, 2, TB, D])
        sqr = sb("sqr", [P, 2, TB, D])
        hb = sb("hb", [P, 2, TB, D])
        inv_cnt = sb("inv_cnt", [P, NT])

        dst_i = sum0[:, 0:S * K].bitcast(I32).rearrange("p (s k) -> p s k", k=K)
        typ_i = sum0[:, S * K:2 * S * K].bitcast(I32).rearrange("p (s k) -> p s k", k=K)
        tbuf = sum1[:, 0:TB * R * D].rearrange("p (b h c) -> p b h c", b=TB, h=2)
        cols0 = last[:, :, :].rearrange("p s k -> p (s k)")[:, 0:2 * TB * P].rearrange(
            "p (b t n) -> p b t n", b=2, t=TB)
        cols1 = onehot[:, :, :].rearrange("p k w -> p (k w)")[:, 0:2 * TB * P].rearrange(
            "p (b t n) -> p b t n", b=2, t=TB)
        hTs = cols1
        ps = ctx.enter_context(nc.psum_tensor("ps", [P, 8, 512], F32))
        ps_t = ps[:, 0:4, :].rearrange("p (b q) c -> p b (q c)", b=2)
        ps_r = ps[:, 4:8, :].rearrange("p (b q) c -> p b q c", b=2)

        s_idx = sem("s_idx")
        s_typ = sem("s_typ")
        s_dst = sem("s_dst")
        s_nxt = sem("s_nxt")
        s_x = sem("s_x")
        s_w = sem("s_w")
        s_fill = sem("s_fill")
        s_v = sem("s_v")
        s_xfill = sem("s_xfill")
        s_nfill = sem("s_nfill")
        s_ends = sem("s_ends")
        s_endsT = sem("s_endsT")
        s_bc = sem("s_bc")
        s_rows = sem("s_rows")
        s_edges = sem("s_edges")
        s_plan = sem("s_plan")
        s_end = sem("s_end")
        s_idx1 = sem("s_idx1")
        s_out = sem("s_out")
        s_sent = [sem(f"s_sent{h}") for h in range(2)]

        def family(prefix, names):
            return {n: sem(f"{prefix}_{n}") for n in names}

        NORM = ["sum", "cen", "sq", "var", "std", "rstd", "norm"]
        FA = family("table", NORM + ["hT", "relu", "rows", "actout", "dveout"])
        FB = family("mid", NORM + ["cols", "sumT", "x1", "cnt", "inv", "h", "hT", "back", "bias", "sign"])
        FC = family("fin", ["cols0", "cols1", "mm", "mean", "base", "res"])
        tstored = [sem(f"tstored{b}") for b in range(TB)]
        hstored = [sem(f"hstored{b}") for b in range(2)]
        LY = [family(f"ly{n}", ["free", "staged", "oh", "win", "acc", "attr", "attr_used"]) for n in range(2)]
        got = [[sem(f"got{n}_{g}") for g in range(NG)] for n in range(2)]
        block = ctx.enter_context(nc.Block())

        xv, outv = (v[0:FULL * NT, :].rearrange("(p t) d -> p t d", t=NT) for v in (x, out))
        t0v = table0.rearrange("(p t r) d -> p t (r d)", t=NT, r=R)
        t1v = table1.rearrange("(p t) d -> p t d", t=NT)
        attrv = edge_attr.rearrange("(s p k) a -> s p (k a)", p=P, k=K)

        def edges(v):
            return v.rearrange("(s p k) -> p s k", p=P, k=K)

        MOST = S * (-(-N // WIN))

        def for_steps(eng, body, before=None, need_first=False):
            with eng.Fori(0, S) as s:
                t0 = eng.value_load(steps[0:1, bass.ds(s, 1), 0], min_val=0, max_val=MOST)
                t1 = eng.value_load(steps[0:1, bass.ds(s, 1), 1], min_val=1, max_val=MOST)
                first = None
                if need_first:
                    first = eng.value_load(steps[0:1, bass.ds(s, 1), 2], min_val=0, max_val=N - 1)
                if before:
                    before(s, t0)
                with eng.Fori(t0, t1) as t:
                    body(s, t, t0, first)

        def gathers(pool, ly, got, table):
            def step(s, t, t0, first):
                for g in range(NG):
                    pool.wait_ge(ly["staged"], t * NG + (g + 1))
                    pool.nop(nofuse=True)
                    for k in range(g * G, g * G + G):
                        pool.indirect_dma_start(
                            msg[:, k, 0:D], None, table,
                            bass.IndirectOffsetOnAxis(ap=istage[:, k:k + 1].bitcast(U32), axis=0)
                        ).then_inc(got[g], 16)
            for_steps(pool, step)

        def stages(act, ly):
            def step(s, t, t0, first):
                for g in range(NG):
                    act.wait_ge(ly["free"], t * NG + (g + 1))
                    act.copy(istage[:, g * G:g * G + G], idx[:, bass.ds(s, 1), g * G:g * G + G].rearrange(
                        "p s k -> p (s k)")).then_inc(ly["staged"], 1)
            for_steps(act, step)

        def products(pe, ly, got, rows):
            def step(s, t, t0, first):
                for g in range(NG):
                    if g == 0:
                        pe.wait_ge(ly["acc"], t + 1)
                    pe.wait_ge(got[g], (t + 1) * (16 * G))
                    pe.wait_ge(ly["oh"], t * NG + (g + 1))
                    for k in range(g * G, g * G + G):
                        mm = pe.matmul(ps[0:rows, 0, 0:WIN], msg[:, k, 0:rows], onehot[:, k, :],
                                       start=(k == 0), stop=(k == K - 1))
                    mm.then_inc(ly["free"], 1)
            for_steps(pe, step)

        def windows(dve, ly, sums, rows):
            def before(s, t0):
                dve.wait_ge(ly["win"], t0 + (s + 1))
                nc.vector.tensor_copy(iota_w[:, :], iota[:, :]).then_inc(ly["win"], 1)

            def step(s, t, t0, first):
                dve.wait_ge(ly["win"], t + (s + 2))
                for g in range(NG):
                    dve.wait_ge(ly["free"], t * NG + (g + 1))
                    if rows > D:
                        if g == 0:
                            dve.wait_ge(ly["attr"], (t + 1) * 16)
                        nc.vector.tensor_tensor(
                            msg[:, g * G:g * G + G, D + 1:M0], attr[:, g * G:g * G + G, :],
                            last[:, bass.ds(s, 1), g * G:g * G + G].rearrange("p s k -> p (s k)").unsqueeze(2)
                            .broadcast_to([P, G, A]), ALU.mult).then_inc(ly["attr_used"], 1)
                    nc.vector.tensor_tensor(
                        onehot[:, g * G:g * G + G, :],
                        iota_w[:, :].unsqueeze(1).broadcast_to([P, G, WIN]),
                        rel[:, bass.ds(s, 1), g * G:g * G + G].rearrange("p s k -> p (s k)").unsqueeze(2)
                        .broadcast_to([P, G, WIN]), ALU.is_equal).then_inc(ly["oh"], 1)
                dve.wait_ge(ly["oh"], t * NG + NG)
                nc.vector.tensor_scalar(iota_w[:, :], iota_w[:, :], float(WIN), None, ALU.add).then_inc(ly["win"], 1)
                dve.wait_ge(ly["free"], t * NG + 2 * NG)
                dve.wait_ge(ly["acc"], t + 1)
                at = nc.s_assert_within(first + (t - t0) * WIN, 0, NN, skip_runtime_bounds_check_because=
                                        "the windows of a superblock start at most at its last node")
                acc = sums[0:rows, bass.ds(at, WIN)]
                nc.vector.tensor_tensor(acc, acc, ps[0:rows, 0, 0:WIN], ALU.add).then_inc(ly["acc"], 1)
            for_steps(dve, step, before, need_first=True)

        def batches(eng, body):
            for n in range(2):
                body(n, n)
            with eng.Fori(1, NB // 2 - 1) as i:
                body(i * 2, 0)
                body(i * 2 + 1, 1)
            for n in range(NB - 2, NB):
                body(n, n % 2)

        def tiles(v, n):
            return v[:, bass.ds(n * TB, TB), :]

        def node_cols(v, r0, r1, n):
            return v[r0:r1, 0:NN].rearrange("r (p t) -> r t p", t=NT)[:, bass.ds(n * TB, TB), :]

        def tile_cols(b, h, c):
            return ps[:, 4 * b + 2 * h:4 * b + 2 * h + 2, :].rearrange("p q c -> p (q c)")[:, 0:TB * P].rearrange(
                "p (t c) -> p t c", c=P)[:, :, 0:c]

        def spread(v):
            return v.unsqueeze(2).broadcast_to([P, TB, D])

        def normalise(dve, f, n, h):
            xin = tiles(x_sb, n)
            dve.nop(nofuse=True)
            nc.vector.tensor_reduce(stat[:, h, 0, :], xin, AX, ALU.add).then_inc(f["sum"], 1)
            dve.wait_ge(f["sum"], n + 1)
            nc.vector.scalar_tensor_tensor(out=cen[:, h], in0=spread(stat[:, h, 0, :]), scalar=-1.0 / D, in1=xin,
                                           op0=ALU.mult, op1=ALU.add).then_inc(f["cen"], 1)
            dve.wait_ge(f["cen"], n + 1)
            if f is FB and n_from(n, 2):
                dve.wait_ge(f["hT"], n - 1)
                dve.wait_ge(hstored[h], (n - h) * 8)
            nc.vector.tensor_tensor(sqr[:, h], cen[:, h], cen[:, h], ALU.mult).then_inc(f["sq"], 1)
            dve.wait_ge(f["sq"], n + 1)
            nc.vector.tensor_reduce(stat[:, h, 1, :], sqr[:, h], AX, ALU.add).then_inc(f["var"], 1)
            dve.wait_ge(f["std"], n + 1)
            nc.vector.reciprocal(stat[:, h, 1, :], stat[:, h, 2, :]).then_inc(f["rstd"], 1)
            dve.wait_ge(f["rstd"], n + 1)
            nc.vector.tensor_tensor(hb[:, h], cen[:, h], spread(stat[:, h, 1, :]), ALU.mult).then_inc(f["norm"], 1)

        def n_from(n, least):
            return not isinstance(n, int) or n >= least

        def deviation(act, f, n, h):
            act.wait_ge(f["var"], n + 1)
            nc.scalar.activation(stat[:, h, 2, :], stat[:, h, 1, :], ACT.Sqrt, bias=eps[:, 0:1],
                                 scale=1.0 / D).then_inc(f["std"], 1)

        @block.gpsimd
        def _(pool):
            nc.gpsimd.iota(iota_i[:, :], pattern=[[1, WIN]], base=0, channel_multiplier=0).then_inc(s_fill, 1)
            nc.gpsimd.iota(iota_c[:, :], pattern=[[0, 1]], base=0, channel_multiplier=1).then_inc(s_fill, 1)
            nc.gpsimd.memset(ones[:, :], 1.0).then_inc(s_fill, 1)
            nc.gpsimd.memset(eps[:, :], EPS).then_inc(s_fill, 1)
            nc.gpsimd.memset(msg[:, :, CNT:CNT + 1], 1.0).then_inc(s_fill, 1)
            pool.wait_ge(s_edges, 1)
            nc.gpsimd.memset(sum0[:, :], 0.0).then_inc(LY[0]["acc"], 1)
            for b in range(TB):
                pool.wait_ge(tstored[b], 16 * NB)
            gathers(pool, LY[0], got[0], table0)
            for b in range(2):
                pool.wait_ge(hstored[b], 8 * NB)
            gathers(pool, LY[1], got[1], table1)

        @block.sync
        def _(sp):
            LOW = P - 32
            sp.dma_start(x_sb[0:LOW], xv[0:LOW]).then_inc(s_x, 16)
            sp.wait_ge(s_xfill, 1)
            sp.dma_start(x_sb[LOW:SPRAY], xv[LOW:SPRAY]).then_inc(s_x, 16)
            sp.dma_start(x_sb[SPRAY:FULL], xv[SPRAY:FULL]).then_inc(s_x, 16)
            sp.dma_start(x_sb[FULL:P, 0:PART, :], x[FULL * NT:N, :].rearrange("(p t) d -> p t d", p=1)).then_inc(s_x, 16)
            sp.dma_start(wrel[0:D], w_rel.rearrange("r f o -> f r o")).then_inc(s_w, 16)
            sp.dma_start(wl[0:D], w_l).then_inc(s_w, 16)
            sp.dma_start(wcomb[0:D], w_r).then_inc(s_w, 16)
            sp.dma_start(wcomb[D:D + 1], b_e.rearrange("(a d) -> a d", a=1)).then_inc(s_w, 16)
            sp.dma_start(wcomb[D + 1:M0], w_e).then_inc(s_w, 16)
            sp.dma_start(bl[:, :], b_l.rearrange("(a d) -> a d", a=1).broadcast_to([P, D])).then_inc(s_w, 16)

            def store_rows(n, h):
                for t in range(TB):
                    sp.wait_ge(FA["actout"], n * TB + (t + 1))
                    sp.wait_ge(FA["dveout"], n * TB + (t + 1))
                    sp.dma_start(t0v[:, bass.ds(n * TB + t, 1), :].rearrange("p t c -> p (t c)"),
                                 tbuf[:, t].rearrange("p h c -> p (h c)")).then_inc(tstored[t], 16)
            batches(sp, store_rows)

            sp.wait_ge(s_plan, 1)

            def load_attr(s, t, t0, first):
                sp.wait_ge(LY[0]["attr_used"], t * NG + 1)
                sp.dma_start(attr[:, :, :].rearrange("p k a -> p (k a)"),
                             attrv[bass.ds(s, 1)].rearrange("s p c -> (s p) c")).then_inc(LY[0]["attr"], 16)
            for_steps(sp, load_attr)

            sp.wait_ge(s_end, 1)
            sp.dma_start(idx[:, :, :], edges(src)).then_inc(s_idx1, 16)
            def store_h(n, h):
                sp.wait_ge(FB["h"], n + 1)
                sp.dma_start(tiles(t1v, n), sqr[:, h]).then_inc(hstored[h], 16)
            batches(sp, store_h)

            def store_out(n, h):
                sp.wait_ge(FC["res"], n + 1)
                o = tiles(outv, n)
                sp.dma_start(o[0:SPRAY], tiles(x_sb, n)[0:SPRAY]).then_inc(s_sent[0], 16)
                sp.dma_start(o[SPRAY:FULL], tiles(x_sb, n)[SPRAY:FULL]).then_inc(s_sent[1], 16)
            batches(sp, store_out)
            sp.dma_start(out[FULL * NT:N, :].rearrange("(p t) d -> p t d", p=1), x_sb[FULL:P, 0:PART, :]).then_inc(s_out, 16)
            for q in s_sent:
                sp.wait_ge(q, 16 * NB)
            sp.wait_ge(s_out, 16)

        @block.scalar
        def _(act):
            act.dma_start(dst_i, edges(dst)).then_inc(s_dst, 16)
            act.wait_ge(s_nfill, 1)
            act.dma_start(nxt[:, 0:S - 1], dst[K:K + (S - 1) * P * K].rearrange("(s p k) -> p s k", p=P, k=K)[:, :, 0:1]
                          .rearrange("p s k -> p (s k)"), allow_slow_non_contiguous=True).then_inc(s_nxt, 16)
            act.dma_start(nxt[0:P - 1, S - 1:S], dst[K + (S - 1) * P * K:E].rearrange("(p k) -> p k", k=K)[:, 0:1],
                          allow_slow_non_contiguous=True).then_inc(s_nxt, 16)
            act.dma_start(idx[:, :, :], edges(src)).then_inc(s_idx, 16)
            act.dma_start(typ_i, edges(edge_type)).then_inc(s_typ, 16)
            act.wait_ge(s_fill, 4)

            def take_rows(n, h):
                for t in range(TB):
                    act.wait_ge(FA["rows"], n * TB + (t + 1))
                    if n_from(n, 1):
                        act.wait_ge(tstored[t], n * 16)
                    nc.scalar.copy(tbuf[:, t, 0], ps[:, 4 + 2 * ((h + t) % 2), :]).then_inc(FA["actout"], 1)

            def table_batch(n, h):
                deviation(act, FA, n, h)
                if n_from(n, 1):
                    take_rows(n - 1, 1 - h)
                act.wait_ge(FA["hT"], n + 1)
                nc.scalar.activation(hTs[0:D, h], tile_cols(0, h, P)[0:D], ACT.Relu).then_inc(FA["relu"], 1)
            batches(act, table_batch)
            take_rows(NB - 1, 1)

            act.wait_ge(s_plan, 1)
            stages(act, LY[0])

            act.wait_ge(s_end, 1)

            def take_cols(n, h):
                if n_from(n, 2):
                    act.wait_ge(FB["sumT"], n - 1)
                nc.scalar.copy(cols0[0:M0, h], node_cols(sum0, 0, M0, n)).then_inc(FB["cols"], 1)
                act.wait_ge(FB["cols"], n + 1)
                cnt_row = node_cols(sum0, CNT, CNT + 1, n)
                nc.scalar.activation(cnt_row, cnt_row, ACT.Sign).then_inc(FB["sign"], 1)

            def put_back(n, h):
                act.wait_ge(FB["hT"], n + 1)
                nc.scalar.copy(node_cols(sum0, 0, D, n), tile_cols(1, h, P)[0:D]).then_inc(FB["back"], 1)

            def mid_batch(n, h):
                if not isinstance(n, int) or n < NB - 1:
                    take_cols(n + 1, 1 - h)
                deviation(act, FB, n, h)
                act.wait_ge(FB["norm"], n + 1)
                nc.scalar.activation(sqr[:, h], hb[:, h], ACT.Relu).then_inc(FB["h"], 1)
                if n_from(n, 1):
                    put_back(n - 1, 1 - h)
            take_cols(0, 0)
            batches(act, mid_batch)
            put_back(NB - 1, 1)

            stages(act, LY[1])

            act.wait_ge(FB["back"], NB)
            act.wait_ge(FB["sign"], NB)

            def final_cols(n, h):
                if n_from(n, 2):
                    act.wait_ge(FC["mm"], n - 1)
                nc.scalar.copy(cols0[0:M0, h], node_cols(sum0, 0, M0, n)).then_inc(FC["cols0"], 1)
            batches(act, final_cols)

        @block.tensor
        def _(pe):
            pe.wait_ge(s_ends, 1)
            pe.transpose(ps[0:S, 0, 0:P], mnp[:, 0:S], ident[:, :])
            pe.transpose(ps[0:S, 1, 0:P], mxp[:, 0:S], ident[:, :]).then_inc(s_endsT, 1)
            pe.wait_ge(s_bc, 2)
            pe.matmul(ps[:, 2, 0:S], bc[0:S, 0, :], ident[0:S, 0:S], start=True, stop=True)
            pe.matmul(ps[:, 3, 0:S], bc[0:S, 1, :], upper[0:S, 0:S], start=True, stop=True)
            pe.matmul(ps[:, 4, 0:S], bc[0:S, 1, :], upper[0:S, 0:S], start=True, stop=False)
            pe.matmul(ps[:, 4, 0:S], bc[0:S, 1, :], ident[0:S, 0:S], start=False, stop=True).then_inc(s_rows, 1)
            pe.wait_ge(s_plan, 1)
            pe.wait_ge(s_w, 16 * 6)

            def rel_rows(n, h):
                pe.wait_ge(FA["relu"], n + 1)
                for t in range(TB):
                    if n_from(n, 1) or t >= 2:
                        pe.wait_ge(FA["actout"], n * TB + (t - 1))
                        pe.wait_ge(FA["dveout"], n * TB + (t - 1))
                    for q in range(2):
                        mm = pe.matmul(ps[:, 4 + 2 * ((h + t) % 2) + q, :], hTs[0:D, h, t, :],
                                       wrel[0:D].rearrange("f r o -> f (r o)")[:, q * HALF:(q + 1) * HALF],
                                       start=True, stop=True)
                    mm.then_inc(FA["rows"], 1)

            def table_batch(n, h):
                if n_from(n, 1):
                    rel_rows(n - 1, 1 - h)
                pe.wait_ge(FA["norm"], n + 1)
                pe.nop(nofuse=True)
                for t in range(TB):
                    mm = pe.transpose(tile_cols(0, h, P)[0:D, t, :], hb[:, h, t, :], ident[:, :])
                mm.then_inc(FA["hT"], 1)
            batches(pe, table_batch)
            rel_rows(NB - 1, 1)

            products(pe, LY[0], got[0], M0)

            def turn_h(n, h):
                pe.wait_ge(FB["h"], n + 1)
                if n_from(n, 2):
                    pe.wait_ge(FB["back"], n - 1)
                pe.nop(nofuse=True)
                for t in range(TB):
                    mm = pe.transpose(tile_cols(1, h, P)[0:D, t, :], sqr[:, h, t, :], ident[:, :])
                mm.then_inc(FB["hT"], 1)

            def mid_batch(n, h):
                pe.wait_ge(FB["cols"], n + 1)
                if n_from(n, 2):
                    pe.wait_ge(FB["cnt"], n - 1)
                    pe.wait_ge(FB["x1"], n - 1)
                for t in range(TB):
                    mm = pe.transpose(tile_cols(0, h, M0)[:, t, :], cols0[0:M0, h, t, :], ident[0:M0, 0:M0])
                mm.then_inc(FB["sumT"], 1)
                if n_from(n, 1):
                    turn_h(n - 1, 1 - h)
            batches(pe, mid_batch)
            turn_h(NB - 1, 1)

            products(pe, LY[1], got[1], D)

            def final_batch(n, h):
                pe.wait_ge(FC["cols0"], n + 1)
                pe.wait_ge(FC["cols1"], n + 1)
                if n_from(n, 2):
                    pe.wait_ge(FC["base"], n - 1)
                for t in range(TB):
                    pe.matmul(ps[:, 2 * h, t * D:t * D + D], cols0[0:M0, h, t, :], wcomb[0:M0, :],
                              start=True, stop=True)
                    mm = pe.matmul(ps[:, 4 + 2 * h, t * D:t * D + D], cols1[0:D, h, t, :], wl[0:D, :],
                                   start=True, stop=True)
                mm.then_inc(FC["mm"], 1)
            batches(pe, final_batch)

        @block.vector
        def _(dve):
            chain = [0]

            def link(ins):
                chain[0] += 1
                ins.then_inc(s_v, 1)
                dve.wait_ge(s_v, chain[0])

            nc.vector.memset(x_sb[P - 32:P, PART:NT, :], 0.0).then_inc(s_xfill, 1)
            nc.vector.memset(nxt[:, :], -1).then_inc(s_nfill, 1)
            dve.wait_ge(s_fill, 5)
            link(nc.vector.tensor_copy(iota[:, :], iota_i[:, :]))
            link(nc.vector.tensor_copy(icol[:, :], iota_c[:, :]))
            link(nc.vector.tensor_scalar(ident[:, :], iota[:, :], icol[:, 0:1], None, ALU.is_equal))
            link(nc.vector.tensor_scalar(upper[:, :], iota[:, :], icol[:, 0:1], None, ALU.is_gt))
            dve.wait_ge(s_dst, 16)
            link(nc.vector.tensor_reduce(mnp[:, :], dst_i, AX, ALU.min))
            nc.vector.tensor_reduce(mxp[:, :], dst_i, AX, ALU.max).then_inc(s_ends, 1)
            dve.wait_ge(s_idx, 16)
            dve.wait_ge(s_typ, 16)
            link(nc.vector.scalar_tensor_tensor(out=idx[:, :, :], in0=idx[:, :, :], scalar=float(R), in1=typ_i,
                                                op0=ALU.mult, op1=ALU.add))
            dve.wait_ge(s_endsT, 1)
            link(nc.vector.tensor_reduce(col[0:S, 0:1], ps[0:S, 0, 0:P], AX, ALU.min))
            link(nc.vector.tensor_reduce(col[0:S, 1:2], ps[0:S, 1, 0:P], AX, ALU.max))
            link(nc.vector.tensor_tensor(coli[0:S, 0:1], col[0:S, 1:2], col[0:S, 0:1], ALU.subtract))
            link(nc.vector.tensor_single_scalar(coli[0:S, 1:2], coli[0:S, 0:1], WIN.bit_length() - 1,
                                                ALU.arith_shift_right))
            link(nc.vector.tensor_scalar(col[0:S, 2:3], coli[0:S, 1:2], 1.0, None, ALU.add))
            nc.vector.tensor_scalar(bc[0:S, 0, :], ones[0:S, :], col[0:S, 0:1], None, ALU.mult).then_inc(s_bc, 1)
            nc.vector.tensor_scalar(bc[0:S, 1, :], ones[0:S, :], col[0:S, 2:3], None, ALU.mult).then_inc(s_bc, 1)
            dve.wait_ge(s_rows, 1)
            link(nc.vector.tensor_copy(steps[0:1, :, 0], ps[0:1, 3, 0:S]))
            link(nc.vector.tensor_copy(steps[0:1, :, 1], ps[0:1, 4, 0:S]))
            link(nc.vector.tensor_copy(steps[0:1, :, 2], ps[0:1, 2, 0:S]))
            link(nc.vector.tensor_tensor(rel[:, :, :], dst_i, ps[:, 2, 0:S].unsqueeze(2).broadcast_to([P, S, K]),
                                         ALU.subtract))
            dve.sem_inc(s_plan, 1)
            dve.wait_ge(s_nxt, 32)
            link(nc.vector.tensor_tensor(last[:, :, 0:K - 1], dst_i[:, :, 0:K - 1], dst_i[:, :, 1:K], ALU.not_equal))
            link(nc.vector.tensor_tensor(last[:, :, K - 1], dst_i[:, :, K - 1], nxt[:, :], ALU.not_equal))
            dve.sem_inc(s_edges, 1)
            dve.sem_inc(LY[0]["free"], NG)
            dve.sem_inc(LY[0]["win"], 1)
            dve.sem_inc(LY[0]["attr_used"], 1)
            dve.wait_ge(s_x, 64)

            def take_rows(n, h):
                for t in range(TB):
                    dve.wait_ge(FA["rows"], n * TB + (t + 1))
                    if n_from(n, 1):
                        dve.wait_ge(tstored[t], n * 16)
                    nc.vector.tensor_copy(tbuf[:, t, 1], ps[:, 5 + 2 * ((h + t) % 2), :]).then_inc(FA["dveout"], 1)

            def table_batch(n, h):
                normalise(dve, FA, n, h)
                if n_from(n, 1):
                    take_rows(n - 1, 1 - h)
            batches(dve, table_batch)
            take_rows(NB - 1, 1)
            for b in range(TB):
                dve.wait_ge(tstored[b], 16 * NB)
            nc.vector.memset(sum1[:, :], 0.0).then_inc(LY[1]["acc"], 1)

            windows(dve, LY[0], sum0, M0)
            n_steps = dve.value_load(steps[0:1, S - 1:S, 1], min_val=1, max_val=MOST)
            dve.wait_ge(LY[0]["acc"], n_steps + 1)
            dve.sem_inc(s_end, 1)

            def mid_batch(n, h):
                dve.wait_ge(FB["sumT"], n + 1)
                sums = tile_cols(0, h, M0)
                nc.vector.tensor_tensor(tiles(x_sb, n), tiles(x_sb, n), sums[:, :, 0:D], ALU.add).then_inc(FB["x1"], 1)
                ic = inv_cnt[:, bass.ds(n * TB, TB)]
                nc.vector.tensor_scalar(ic, sums[:, :, CNT], 1.0, None, ALU.max).then_inc(FB["cnt"], 1)
                dve.wait_ge(FB["x1"], n + 1)
                if n_from(n, 2):
                    dve.wait_ge(FB["h"], n - 1)
                normalise(dve, FB, n, h)
                nc.vector.tensor_tensor(tiles(x_sb, n), tiles(x_sb, n),
                                        bl[:, :].unsqueeze(1).broadcast_to([P, TB, D]), ALU.add).then_inc(FB["bias"], 1)
            batches(dve, mid_batch)
            dve.wait_ge(FB["cnt"], NB)
            nc.vector.reciprocal(inv_cnt[:, :], inv_cnt[:, :]).then_inc(FB["inv"], 1)
            dve.wait_ge(s_idx1, 16)
            dve.sem_inc(LY[1]["free"], NG)
            dve.sem_inc(LY[1]["win"], 1)

            windows(dve, LY[1], sum1, D)
            dve.wait_ge(LY[1]["acc"], n_steps + 1)
            dve.wait_ge(FB["bias"], NB)
            dve.wait_ge(FB["inv"], 1)

            def results(n, h):
                dve.wait_ge(FC["mm"], n + 1)
                row = sqr[:, h]
                nc.vector.tensor_tensor(row, ps[:, 4 + 2 * h, 0:TB * D].rearrange("p (t d) -> p t d", d=D),
                                        spread(inv_cnt[:, bass.ds(n * TB, TB)]), ALU.mult).then_inc(FC["mean"], 1)
                dve.wait_ge(FC["mean"], n + 1)
                nc.vector.tensor_tensor(row, row, ps[:, 2 * h, 0:TB * D].rearrange("p (t d) -> p t d", d=D),
                                        ALU.add).then_inc(FC["base"], 1)
                dve.wait_ge(FC["base"], n + 1)
                nc.vector.tensor_tensor(tiles(x_sb, n), tiles(x_sb, n), row, ALU.add).then_inc(FC["res"], 1)

            def final_batch(n, h):
                nc.vector.tensor_copy(cols1[0:D, h], node_cols(sum1, 0, D, n)).then_inc(FC["cols1"], 1)
                if n_from(n, 1):
                    results(n - 1, 1 - h)
            batches(dve, final_batch)
            results(NB - 1, 1)


def kernel(**inputs):
    import numpy as np
    import concourse.bacc as bacc
    from concourse.bass_utils import run_bass_kernel_spmd

    names = ["x", "src", "dst", "edge_attr_16", "edge_type_16", "L0_gnn_weight", "L1_gnn_W_l", "L1_gnn_b_l",
             "L1_gnn_W_r", "L1_gnn_W_e", "L1_gnn_b_e"]
    nc = bacc.Bacc("TRN2", target_bir_lowering=False, num_devices=1)
    arrays, args = {}, []
    for name in names:
        a = np.ascontiguousarray(inputs[name])
        arrays[f"in_{name}"] = a
        args.append(nc.dram_tensor(f"in_{name}", a.shape, mybir.dt.from_np(a.dtype), kind="ExternalInput").ap())
    out = nc.dram_tensor("out_x", inputs["x"].shape, F32, kind="ExternalOutput").ap()
    gnn_two_layers(nc, *args, out)
    r = run_bass_kernel_spmd(nc, [arrays], core_ids=[0])
    return r.results[0]["out_x"]
```
